# Optimizing a Trainium2 kernel written in Bass

```python
import numpy as np
import jax
import jax.numpy as jnp

def _softmax(x, axis=-1):
    return jax.nn.softmax(x, axis=axis)

def _gelu(x):
    return jax.nn.gelu(x, approximate=True)

def _silu(x):
    return jax.nn.silu(x)

def _sigmoid(x):
    return jax.nn.sigmoid(x)

def _layernorm(x, axis=-1, eps=1e-05):
    m = jnp.mean(x, axis=axis, keepdims=True)
    v = jnp.var(x, axis=axis, keepdims=True)
    return (x - m) / jnp.sqrt(v + eps)

def _scatter_add(tgt, idx, src, axis=0):
    return tgt.at[idx].add(src)

def _segment_sum(src, seg, n):
    return jax.ops.segment_sum(src, seg, n)
kernel_name = 'mk_adj_resnorm_d1_adj_r2_4d41e1'

def setup_inputs(seed: int=0):
    np.random.seed(seed)
    _w = jnp.asarray

    def _rec_inputs():
        import jax
        import jax.numpy as jnp
        _gk = jax.random.key(seed)
        x = -0.003407 + 1.001 * jax.random.normal(jax.random.fold_in(_gk, 1), (64, 128, 64), jnp.float32)
        _w = (1.0 + jnp.arange(128, dtype=jnp.float32)) ** (-0.5)
        _w = _w / _w.mean()
        _pij = jnp.clip(0.125 * _w[:, None] * _w[None, :], 0.0, 1.0)
        _a = jax.random.uniform(jax.random.fold_in(_gk, 2), (64, 128, 128)) < _pij
        _a = jnp.logical_or(_a, jnp.swapaxes(_a, -1, -2))
        _a = jnp.logical_or(_a, jnp.eye(128, dtype=bool))
        _af = _a.astype(jnp.float32)
        _af = _af * jax.random.uniform(jax.random.fold_in(_gk, 3), (64, 128, 128), jnp.float32, 0.05, 0.999994)
        adj = _af
        return (x, adj)
    x, adj = _rec_inputs()

    def _L0_gnn_setup():
        import jax, jax.numpy as jnp
        import numpy as np
        B, N, F_IN, H = (4, 256, 64, 128)
        key = jax.random.key(seed)
        ks = jax.random.split(key, 14)
        s = lambda fan_in: 1.0 / np.sqrt(fan_in)
        inp = {'x': jax.random.normal(ks[0], (B, N, F_IN), dtype=jnp.float32), 'adj': jax.random.uniform(ks[1], (B, N, N), dtype=jnp.float32), 'skip_conn': 0, 'W_e1': jax.random.uniform(ks[2], (2 * F_IN, H), minval=-s(2 * F_IN), maxval=s(2 * F_IN)), 'b_e1': jax.random.uniform(ks[3], (H,), minval=-s(2 * F_IN), maxval=s(2 * F_IN)), 'W_e2': jax.random.uniform(ks[4], (H, H), minval=-s(H), maxval=s(H)), 'b_e2': jax.random.uniform(ks[5], (H,), minval=-s(H), maxval=s(H)), 'W_n1': jax.random.uniform(ks[6], (H, H), minval=-s(H), maxval=s(H)), 'b_n1': jax.random.uniform(ks[7], (H,), minval=-s(H), maxval=s(H)), 'W_n2': jax.random.uniform(ks[8], (H, H), minval=-s(H), maxval=s(H)), 'b_n2': jax.random.uniform(ks[9], (H,), minval=-s(H), maxval=s(H)), 'W_out': jax.random.uniform(ks[10], (F_IN + H, F_IN), minval=-s(F_IN + H), maxval=s(F_IN + H)), 'b_out': jax.random.uniform(ks[11], (F_IN + H,), minval=-s(F_IN + H), maxval=s(F_IN + H))[:F_IN]}
        return inp
    _L0_gnn_all = _L0_gnn_setup()
    _L0_gnn_in = {k: v for k, v in _L0_gnn_all.items() if k in ('W_e1', 'b_e1', 'W_e2', 'b_e2', 'W_n1', 'b_n1', 'W_n2', 'b_n2', 'W_out', 'b_out')}
    del _L0_gnn_all
    return {'x': x, 'adj': adj, 'L0_gnn_W_e1': _L0_gnn_in['W_e1'], 'L0_gnn_b_e1': _L0_gnn_in['b_e1'], 'L0_gnn_W_e2': _L0_gnn_in['W_e2'], 'L0_gnn_b_e2': _L0_gnn_in['b_e2'], 'L0_gnn_W_n1': _L0_gnn_in['W_n1'], 'L0_gnn_b_n1': _L0_gnn_in['b_n1'], 'L0_gnn_W_n2': _L0_gnn_in['W_n2'], 'L0_gnn_b_n2': _L0_gnn_in['b_n2'], 'L0_gnn_W_out': _L0_gnn_in['W_out'], 'L0_gnn_b_out': _L0_gnn_in['b_out']}

def reference(x, adj, L0_gnn_W_e1, L0_gnn_b_e1, L0_gnn_W_e2, L0_gnn_b_e2, L0_gnn_W_n1, L0_gnn_b_n1, L0_gnn_W_n2, L0_gnn_b_n2, L0_gnn_W_out, L0_gnn_b_out):
    import jax
    import jax.numpy as jnp

    def _L0_gnn_ref(x, adj, skip_conn, W_e1, b_e1, W_e2, b_e2, W_n1, b_n1, W_n2, b_n2, W_out, b_out):
        import jax, jax.numpy as jnp
        import numpy as np
        B, N, F_IN, H = (4, 256, 64, 128)
        n = adj.shape[1]
        innode = jnp.broadcast_to(x[:, None, :, :], (x.shape[0], n, n, x.shape[-1]))
        outnode = jnp.broadcast_to(x[:, :, None, :], (x.shape[0], n, n, x.shape[-1]))
        e_in = jnp.concatenate([innode, outnode], axis=-1)
        node2edge = jax.nn.relu(e_in @ W_e1 + b_e1)
        edge2edge = jax.nn.relu(node2edge @ W_e2 + b_e2)
        out = jnp.einsum('bij,bijh->bjh', adj, edge2edge)
        out = jax.nn.relu(out @ W_n1 + b_n1)
        out = jax.nn.relu(out @ W_n2 + b_n2)
        out = jnp.concatenate([x, out], axis=-1) @ W_out + b_out
        if skip_conn == 1:
            out = out + x
        return out
    x = _layernorm(x + _L0_gnn_ref(x, adj, 0, L0_gnn_W_e1, L0_gnn_b_e1, L0_gnn_W_e2, L0_gnn_b_e2, L0_gnn_W_n1, L0_gnn_b_n1, L0_gnn_W_n2, L0_gnn_b_n2, L0_gnn_W_out, L0_gnn_b_out), axis=-1)
    return x

_drawn_inputs = setup_inputs


def setup_inputs(seed=0):
    import zlib

    import numpy as np

    out = dict(_drawn_inputs(seed))
    spreads = {}
    factors = {'L0_gnn_b_e1': 4.353, 'L0_gnn_b_n1': 8.0, 'L0_gnn_b_n2': 3.846}
    for name, (base, spread) in spreads.items():
        noise = np.random.default_rng([zlib.crc32(name.encode()), seed]).standard_normal(out[name].shape)
        drawn = base * np.exp(spread * noise) if base else spread * noise
        out[name] = jnp.asarray(drawn.astype(out[name].dtype))
    for name, factor in factors.items():
        out[name] = (out[name] * factor).astype(out[name].dtype)
    return out
```

```python
from contextlib import ExitStack

import concourse.bass as bass
from concourse import mybir

ALU = mybir.AluOpType
ACT = mybir.ActivationFunctionType
F32 = mybir.dt.float32
BF16 = mybir.dt.bfloat16

TJ = 8
BANK = 512
RING = 4
Z_AHEAD = 2
Y_AHEAD = 3
PARTS = 3
DMA = 16
LN_EPS = 1e-5

PE_NODE1, PE_NODE2, PE_OUT, PE_UV = 2, 6, 9, 7
ACT_NODE1, ACT_NODE2, ACT_SQRT = 5, 8, 13
DVE_CUT, DVE_UV, DVE_NORM1, DVE_NORM2 = 3, 8, 11, 14
POOL_RESIDUAL = 8


def build_gnn(nc, x, x_t, adj_t, w_e1, b_e1, w_e2, b_e2, w_n1, b_n1, w_n2, b_n2, w_out, b_out, out):
    B, N, F = x.shape
    H = w_e2.shape[0]
    TILES = N // TJ
    HALF = BANK // N
    ROWS = N // 2
    assert N == 128 and H == 128 and 2 * F == w_e1.shape[0] and TJ == 2 * HALF
    assert TILES % RING == 0 and TILES % 2 == 0

    with ExitStack() as ctx:
        def sb(name, shape, dt=F32):
            return ctx.enter_context(nc.sbuf_tensor(name, shape, dt))

        def ps(name, shape):
            return ctx.enter_context(nc.psum_tensor(name, shape, F32))

        def sem(name):
            return ctx.enter_context(nc.semaphore(name))

        w_u = sb("w_u", [F, H])
        w_v = sb("w_v", [F, H])
        w_e2_sb = sb("w_e2_sb", [H, H])
        w_n1_sb = sb("w_n1_sb", [H, H])
        w_n2_sb = sb("w_n2_sb", [H, H])
        w_out_x = sb("w_out_x", [F, F])
        w_out_h = sb("w_out_h", [H, F])
        b_uv = sb("b_uv", [H, 2])
        b_e2_sb = sb("b_e2_sb", [H, 1])
        b_n1_sb = sb("b_n1_sb", [H, 1])
        b_n2_sb = sb("b_n2_sb", [H, 1])
        b_out_sb = sb("b_out_sb", [N, F])
        ones = sb("ones", [PARTS, H], BF16)
        x_uv = sb("x_uv", [F, N])
        x_out = sb("x_out", [F, N])
        x_nat = sb("x_nat", [N, F])
        x_bias = sb("x_bias", [N, F])
        uv_next = sb("uv_next", [H, 2, N])
        uv = sb("uv", [H, 2, N])
        y_ring = sb("y_ring", [H, RING, TJ, N])
        e_ring = sb("e_ring", [H, RING, TJ, N])
        adj_blk = sb("adj_blk", [N, N])
        adj_rest = sb("adj_rest", [N, N])
        adj_parts = sb("adj_parts", [N, PARTS, N], BF16)
        adj_rows = sb("adj_rows", [PARTS, N * N], BF16)
        agg = sb("agg", [H, N])
        agg_full = sb("agg_full", [H, N])
        node1 = sb("node1", [H, N])
        node2 = sb("node2", [H, N])
        res = sb("res", [N, F])
        y_out = sb("y_out", [N, F])
        dev = sb("dev", [N, F])
        total = sb("total", [N, 1])
        mean = sb("mean", [N, 1])
        squares = sb("squares", [N, 1])
        var4 = sb("var4", [N, 1])
        std2 = sb("std2", [N, 1])
        inv2 = sb("inv2", [N, 1])
        std = sb("std", [N, 1])
        rstd = sb("rstd", [N, 1])
        root_in = sb("root_in", [N, 1])

        z_ps = ps("z_ps", [H, 2, TJ * N])
        a_ps = ps("a_ps", [H, 2, BANK])
        node_ps = ps("node_ps", [H, BANK])
        uv_ps = ps("uv_ps", [H, BANK])

        weights_in = sem("weights_in")
        ones_set = sem("ones_set")
        u_bias_set = sem("u_bias_set")
        root_in_set = sem("root_in_set")
        x_uv_in = sem("x_uv_in")
        x_out_in = sem("x_out_in")
        x_nat_in = sem("x_nat_in")
        adj_in = sem("adj_in")
        cut_step = sem("cut_step")
        rows_in = [sem("rows_in_0"), sem("rows_in_1")]
        uv_done = sem("uv_done")
        uv_saved = sem("uv_saved")
        uv_taken = sem("uv_taken")
        y_sum = sem("y_sum")
        y_ready = sem("y_ready")
        z_ready = sem("z_ready")
        e_ready = sem("e_ready")
        a_ready = sem("a_ready")
        agg_done = sem("agg_done")
        agg_saved = sem("agg_saved")
        node_mm = sem("node_mm")
        node_act = sem("node_act")
        res_bias = sem("res_bias")
        norm_step = sem("norm_step")
        root_done = sem("root_done")
        y_out_free = sem("y_out_free")

        NORM = 9
        ROOT_AT = 5
        WEIGHTS = 12

        block = ctx.enter_context(nc.Block())

        def batches(eng, body):
            body(0, first=True)
            with eng.Fori(1, B - 1) as b:
                body(b)
            body(B - 1, last=True)

        @block.sync
        def _(sp):
            sp.dma_start(x_uv[:], x_t[:, 0, :]).then_inc(x_uv_in, DMA)
            sp.dma_start(adj_blk[:], adj_t[0]).then_inc(adj_in, DMA)
            for dst, src in (
                (w_u, w_e1[0:F]), (w_v, w_e1[F:2 * F]), (w_e2_sb, w_e2), (w_n1_sb, w_n1),
                (w_n2_sb, w_n2), (w_out_x, w_out[0:F]), (w_out_h, w_out[F:F + H]),
                (b_uv[:, 0:1], b_e1), (b_e2_sb, b_e2), (b_n1_sb, b_n1), (b_n2_sb, b_n2),
                (b_out_sb, b_out.partition_broadcast(N)),
            ):
                sp.dma_start(dst if isinstance(dst, bass.AP) else dst[:], src).then_inc(weights_in, DMA)

            def rows(b, half):
                sp.wait_ge(cut_step, 4 * b + 4)
                for part in range(PARTS):
                    dst = adj_rows[part:part + 1, half * ROWS * N:(half + 1) * ROWS * N]
                    sp.dma_start(dst.rearrange("p (j i) -> p j i", i=N),
                                 adj_parts[half * ROWS:(half + 1) * ROWS, part, :]
                                 ).then_inc(rows_in[half], DMA)

            def store(b):
                sp.wait_ge(norm_step, NORM * b + NORM)
                sp.dma_start(out[b], y_out[:]).then_inc(y_out_free, DMA)

            rows(0, 0)
            rows(0, 1)

            def body(b, first=False, last=False):
                if not last:
                    sp.wait_ge(uv_done, b + 1)
                    sp.dma_start(x_uv[:], x_t[:, b + 1, :]).then_inc(x_uv_in, DMA)
                    sp.wait_ge(cut_step, 4 * b + 4)
                    sp.dma_start(adj_blk[:], adj_t[b + 1]).then_inc(adj_in, DMA)
                    sp.wait_ge(a_ready, 2 * TILES * b + TILES)
                    rows(b + 1, 0)
                if not first:
                    sp.wait_ge(node_mm, 3 * b)
                    sp.wait_ge(res_bias, b)
                sp.dma_start(x_out[:], x_t[:, b, :]).then_inc(x_out_in, DMA)
                sp.dma_start(x_nat[:], x[b]).then_inc(x_nat_in, DMA)
                if not first:
                    store(b - 1)
                if not last:
                    sp.wait_ge(a_ready, 2 * TILES * b + 2 * TILES)
                    rows(b + 1, 1)

            batches(sp, body)
            store(B - 1)
            sp.wait_ge(y_out_free, DMA * (B + 1))

        @block.gpsimd
        def _(pool):
            nc.gpsimd.memset(ones[:], 1.0).then_inc(ones_set, 1)
            nc.gpsimd.memset(b_uv[:, 1:2], 0.0).then_inc(u_bias_set, 1)
            pool.wait_ge(u_bias_set, 1)
            pool.wait_ge(weights_in, DMA * WEIGHTS)

            def residual(b):
                pool.wait_ge(x_nat_in, DMA * b + DMA)
                pool.wait_ge(agg_saved, b + 1)
                nc.gpsimd.tensor_tensor(x_bias[:], x_nat[:], b_out_sb[:], ALU.add).then_inc(res_bias, 1)

            def body(b, first=False, last=False):
                pool.wait_ge(uv_saved, b + 1)
                if not first:
                    pool.wait_ge(y_sum, TILES * b)
                nc.gpsimd.tensor_tensor(uv[:], uv_next[:], b_uv[:].unsqueeze(2).broadcast_to([H, 2, N]),
                                        ALU.add).then_inc(uv_taken, 1)
                pool.wait_ge(uv_taken, b + 1)
                for t in range(TILES):
                    if not (first and t < RING):
                        pool.wait_ge(z_ready, TILES * b + t - RING + 1)
                    v = uv[:, 0, :].unsqueeze(1).broadcast_to([H, TJ, N])
                    u = uv[:, 1, TJ * t:TJ * t + TJ].unsqueeze(2).broadcast_to([H, TJ, N])
                    nc.gpsimd.tensor_tensor(y_ring[:, t % RING], v, u, ALU.add).then_inc(y_sum, 1)
                    if t == POOL_RESIDUAL and not first:
                        residual(b - 1)

            batches(pool, body)
            residual(B - 1)

        @block.scalar
        def _(act):
            act.wait_ge(root_in_set, 1)
            nc.scalar.activation(root_in[:], root_in[:], ACT.Sqrt)
            act.wait_ge(weights_in, DMA * WEIGHTS)

            def relu_y(b, t):
                slot = y_ring[:, t % RING]
                act.wait_ge(y_sum, TILES * b + t + 1)
                nc.scalar.activation(slot, slot, ACT.Relu).then_inc(y_ready, 1)

            def relu_e(b, t, first):
                act.wait_ge(z_ready, TILES * b + t + 1)
                if not (first and t < RING):
                    act.wait_ge(agg_done, 2 * (TILES * b + t - RING + 1))
                nc.scalar.activation(e_ring[:, t % RING].rearrange("p j i -> p (j i)"), z_ps[:, t % 2],
                                     ACT.Relu, bias=b_e2_sb[:]).then_inc(e_ready, 1)

            def node_relu(b, layer):
                dst, bias = ((node1, b_n1_sb), (node2, b_n2_sb))[layer]
                act.wait_ge(node_mm, 3 * b + layer + 1)
                nc.scalar.activation(dst[:], node_ps[:, 0:N], ACT.Relu, bias=bias[:]).then_inc(node_act, 1)

            def root(b):
                act.wait_ge(norm_step, NORM * b + ROOT_AT)
                nc.scalar.activation(std2[:], var4[:], ACT.Sqrt).then_inc(root_done, 1)

            def body(b, first=False, last=False):
                for t in range(TILES):
                    relu_e(b, t, first)
                    if not (last and t + Y_AHEAD >= TILES):
                        relu_y(b, t + Y_AHEAD)
                    if not first:
                        if t == ACT_NODE1:
                            node_relu(b - 1, 0)
                        if t == ACT_NODE2:
                            node_relu(b - 1, 1)
                        if t == ACT_SQRT:
                            root(b - 1)

            for t in range(Y_AHEAD):
                relu_y(0, t)
            batches(act, body)
            node_relu(B - 1, 0)
            node_relu(B - 1, 1)
            root(B - 1)

        @block.vector
        def _(dve):
            nc.vector.memset(root_in[:], 1.0).then_inc(root_in_set, 1)
            nc.vector.memset(y_out[:], 0.0).then_inc(y_out_free, DMA)
            dve.wait_ge(weights_in, DMA * WEIGHTS)

            def cut(b, step, whole=False):
                hi, mid, lo = (adj_parts[:, part, :] for part in range(PARTS))
                if step == 0:
                    dve.wait_ge(adj_in, DMA * b + DMA)
                    if not whole:
                        for half in range(2):
                            dve.wait_ge(rows_in[half], DMA * PARTS * b)
                    ins = nc.vector.tensor_copy(hi, adj_blk[:])
                if step == 1:
                    dve.wait_ge(cut_step, 4 * b + 1)
                    ins = nc.vector.tensor_tensor(adj_rest[:], adj_blk[:], hi, ALU.subtract)
                if step == 2:
                    dve.wait_ge(cut_step, 4 * b + 2)
                    ins = nc.vector.tensor_copy(mid, adj_rest[:])
                if step == 3:
                    dve.wait_ge(cut_step, 4 * b + 3)
                    ins = nc.vector.tensor_tensor(lo, adj_rest[:], mid, ALU.subtract)
                ins.then_inc(cut_step, 1)

            def save_uv(b, first=False):
                dve.wait_ge(uv_done, b + 1)
                if not first:
                    dve.wait_ge(uv_taken, b)
                nc.vector.tensor_copy(uv_next[:].rearrange("p s i -> p (s i)"), uv_ps[:, 0:2 * N]
                                      ).then_inc(uv_saved, 1)

            def aggregate(b, t, first):
                dve.wait_ge(e_ready, TILES * b + t + 1)
                if t == 0 and not first:
                    dve.wait_ge(agg_saved, b)
                for half in range(2):
                    dve.wait_ge(a_ready, 2 * (TILES * b + t) + half + 1)
                    for k in range(HALF):
                        e = e_ring[:, t % RING, half * HALF + k, :]
                        j = t * TJ + half * HALF + k
                        ins = nc.vector.tensor_tensor_reduce(
                            e, e, a_ps[:, half, k * N:(k + 1) * N], 1.0, 0.0, ALU.mult, ALU.add,
                            agg[:, j:j + 1])
                    ins.then_inc(agg_done, 1)

            def save_agg(b, first):
                dve.wait_ge(agg_done, 2 * TILES * b + 2 * TILES)
                if not first:
                    dve.wait_ge(node_mm, 3 * b)
                nc.vector.tensor_copy(agg_full[:], agg[:]).then_inc(agg_saved, 1)

            def norm1(b):
                at = NORM * b
                dve.wait_ge(node_mm, 3 * b + 3)
                dve.wait_ge(res_bias, b + 1)
                nc.vector.scalar_tensor_tensor(out=res[:], in0=node_ps[:, 0:F], scalar=0.0, in1=x_bias[:],
                                               op0=ALU.add, op1=ALU.add, accum_out=total[:]
                                               ).then_inc(norm_step, 1)
                dve.wait_ge(norm_step, at + 1)
                nc.vector.tensor_scalar(mean[:], total[:], 1.0 / F, None, ALU.mult).then_inc(norm_step, 1)
                dve.wait_ge(norm_step, at + 2)
                nc.vector.tensor_scalar(dev[:], res[:], mean[:], None, ALU.subtract).then_inc(norm_step, 1)
                dve.wait_ge(norm_step, at + 3)
                nc.vector.scalar_tensor_tensor(out=res[:], in0=dev[:], scalar=1.0, in1=dev[:],
                                               op0=ALU.mult, op1=ALU.mult, accum_out=squares[:]
                                               ).then_inc(norm_step, 1)
                dve.wait_ge(norm_step, at + 4)
                nc.vector.tensor_scalar(var4[:], squares[:], 0.25 / F, 0.25 * LN_EPS, ALU.mult,
                                        ALU.add).then_inc(norm_step, 1)

            def norm2(b):
                at = NORM * b
                dve.wait_ge(root_done, b + 1)
                nc.vector.reciprocal(inv2[:], std2[:]).then_inc(norm_step, 1)
                dve.wait_ge(norm_step, at + 6)
                nc.vector.scalar_tensor_tensor(out=std[:], in0=var4[:], scalar=inv2[:], in1=std2[:],
                                               op0=ALU.mult, op1=ALU.add).then_inc(norm_step, 1)
                dve.wait_ge(norm_step, at + 7)
                nc.vector.reciprocal(rstd[:], std[:]).then_inc(norm_step, 1)
                dve.wait_ge(norm_step, at + 8)
                dve.wait_ge(y_out_free, DMA * (b + 1))
                nc.vector.tensor_scalar(y_out[:], dev[:], rstd[:], None, ALU.mult).then_inc(norm_step, 1)

            def body(b, first=False, last=False):
                for t in range(TILES):
                    aggregate(b, t, first)
                    if not last:
                        if 0 <= t - DVE_CUT < 4:
                            cut(b + 1, t - DVE_CUT)
                        if t == DVE_UV:
                            save_uv(b + 1)
                    if not first:
                        if t == DVE_NORM1:
                            norm1(b - 1)
                        if t == DVE_NORM2:
                            norm2(b - 1)
                save_agg(b, first)

            for step in range(4):
                cut(0, step, whole=True)
            save_uv(0, first=True)
            batches(dve, body)
            norm1(B - 1)
            norm2(B - 1)

        @block.tensor
        def _(pe):
            pe.wait_ge(weights_in, DMA * WEIGHTS)
            pe.wait_ge(ones_set, 1)

            def uv_products(b, first=False):
                pe.wait_ge(x_uv_in, DMA * b + DMA)
                if not first:
                    pe.wait_ge(uv_saved, b)
                nc.tensor.matmul(uv_ps[:, 0:N], w_v[:], x_uv[:], start=True, stop=True)
                nc.tensor.matmul(uv_ps[:, N:2 * N], w_u[:], x_uv[:], start=True, stop=True
                                 ).then_inc(uv_done, 1)

            def z_half(b, t, half, first=False):
                if half == 0:
                    pe.wait_ge(y_ready, TILES * b + t + 1)
                    if not (first and t < 2):
                        pe.wait_ge(e_ready, TILES * b + t - 1)
                y = y_ring[:, t % RING, half * HALF:(half + 1) * HALF, :].rearrange("p j i -> p (j i)")
                mm = nc.tensor.matmul(z_ps[:, t % 2, half * BANK:(half + 1) * BANK], w_e2_sb[:], y,
                                      start=True, stop=True)
                if half == 1:
                    mm.then_inc(z_ready, 1)

            def spread(b, t, half, first):
                if t % (TILES // 2) == 0 and half == 0:
                    pe.wait_ge(rows_in[2 * t // TILES], DMA * PARTS * (b + 1))
                if not (first and t == 0):
                    pe.wait_ge(agg_done, 2 * (TILES * b + t) + half - 1)
                at = (t * TJ + half * HALF) * N
                nc.tensor.matmul(a_ps[:, half, :], ones[:], adj_rows[:, at:at + BANK], start=True,
                                 stop=True).then_inc(a_ready, 1)

            def node_product(b, layer):
                if layer == 0:
                    pe.wait_ge(agg_saved, b + 1)
                    nc.tensor.matmul(node_ps[:, 0:N], w_n1_sb[:], agg_full[:], start=True, stop=True
                                     ).then_inc(node_mm, 1)
                if layer == 1:
                    pe.wait_ge(node_act, 2 * b + 1)
                    nc.tensor.matmul(node_ps[:, 0:N], w_n2_sb[:], node1[:], start=True, stop=True
                                     ).then_inc(node_mm, 1)
                if layer == 2:
                    pe.wait_ge(node_act, 2 * b + 2)
                    pe.wait_ge(x_out_in, DMA * b + DMA)
                    nc.tensor.matmul(node_ps[:, 0:F], x_out[:], w_out_x[:], start=True, stop=False)
                    nc.tensor.matmul(node_ps[:, 0:F], node2[:], w_out_h[:], start=False, stop=True
                                     ).then_inc(node_mm, 1)

            def body(b, first=False, last=False):
                for t in range(TILES):
                    for half in range(2):
                        if not (last and t + Z_AHEAD >= TILES):
                            z_half(b, t + Z_AHEAD, half)
                        spread(b, t, half, first)
                    if not first:
                        for layer, at in enumerate((PE_NODE1, PE_NODE2, PE_OUT)):
                            if t == at:
                                node_product(b - 1, layer)
                    if not last and t == PE_UV:
                        uv_products(b + 1)

            uv_products(0, first=True)
            for t in range(Z_AHEAD):
                for half in range(2):
                    z_half(0, t, half, first=True)
            batches(pe, body)
            for layer in range(3):
                node_product(B - 1, layer)


def kernel(x, adj, L0_gnn_W_e1, L0_gnn_b_e1, L0_gnn_W_e2, L0_gnn_b_e2, L0_gnn_W_n1, L0_gnn_b_n1,
           L0_gnn_W_n2, L0_gnn_b_n2, L0_gnn_W_out, L0_gnn_b_out):
    import numpy as np
    import concourse.bacc as bacc
    from concourse.bass_utils import run_bass_kernel_spmd

    def laid(a):
        return np.ascontiguousarray(a)

    def column(a):
        return laid(np.asarray(a).reshape(-1, 1))

    x, adj = np.asarray(x), np.asarray(adj)
    arrays = {
        "x": laid(x),
        "x_t": laid(x.transpose(2, 0, 1)),
        "adj_t": laid(adj.transpose(0, 2, 1)),
        "w_e1": laid(L0_gnn_W_e1), "b_e1": column(L0_gnn_b_e1),
        "w_e2": laid(L0_gnn_W_e2), "b_e2": column(L0_gnn_b_e2),
        "w_n1": laid(L0_gnn_W_n1), "b_n1": column(L0_gnn_b_n1),
        "w_n2": laid(L0_gnn_W_n2), "b_n2": column(L0_gnn_b_n2),
        "w_out": laid(L0_gnn_W_out), "b_out": laid(L0_gnn_b_out),
    }
    nc = bacc.Bacc("TRN2", target_bir_lowering=False, num_devices=1)
    args = [nc.dram_tensor(name, a.shape, mybir.dt.from_np(a.dtype), kind="ExternalInput").ap()
            for name, a in arrays.items()]
    out = nc.dram_tensor("out", x.shape, F32, kind="ExternalOutput").ap()
    build_gnn(nc, *args, out)
    result = run_bass_kernel_spmd(nc, [arrays], core_ids=[0])
    return result.results[0]["out"]
```

```python
from contextlib import ExitStack

import concourse.bass as bass
from concourse import mybir

ALU = mybir.AluOpType
ACT = mybir.ActivationFunctionType
F32 = mybir.dt.float32
BF16 = mybir.dt.bfloat16

TJ = 8
BANK = 512
Y_RING = 4
Y_AHEAD = 3
CHUNKS = 4
PARTS = 3
DMA = 16
LN_EPS = 1e-5

PE_UV, PE_NODE = 1, (2, 3, 4)
ACT_NODE1, ACT_NODE2, ACT_ROOT = 7, 9, 15
DVE_UV = 7
DVE_CUT = (8, 10, 12, 14)
DVE_NORM = (20, 21, 22, 23, 24, 28, 29, 30, 31)
DVE_RELU = {5: 6, 21: 14}
POOL_RESIDUAL = 8


def build_gnn(nc, x, x_t, adj_t, w_e1, b_e1, w_e2, b_e2, w_n1, b_n1, w_n2, b_n2, w_out, b_out, out):
    B, N, F = x.shape
    H = w_e2.shape[0]
    TILES = N // TJ
    PAIRS = TILES // 2
    HALF = BANK // N
    SPREAD = N // 2
    ROWS = SPREAD // 2
    CHUNK = (N - SPREAD) // CHUNKS
    Y_BY_DVE = sorted(DVE_RELU.values())
    Y_BY_ACT = TILES - len(Y_BY_DVE)
    assert N == 128 and H == 128 and 2 * F == w_e1.shape[0] and TJ == 2 * HALF
    assert TILES % Y_RING == 0 and PAIRS % 4 == 0 and CHUNK % TJ == 0

    with ExitStack() as ctx:
        def sb(name, shape, dt=F32):
            return ctx.enter_context(nc.sbuf_tensor(name, shape, dt))

        def ps(name, shape):
            return ctx.enter_context(nc.psum_tensor(name, shape, F32))

        def sem(name):
            return ctx.enter_context(nc.semaphore(name))

        w_u = sb("w_u", [F, H])
        w_v = sb("w_v", [F, H])
        w_e2_sb = sb("w_e2_sb", [H, H])
        w_n1_sb = sb("w_n1_sb", [H, H])
        w_n2_sb = sb("w_n2_sb", [H, H])
        w_out_x = sb("w_out_x", [F, F])
        w_out_h = sb("w_out_h", [H, F])
        b_uv = sb("b_uv", [H, 2])
        b_e2_sb = sb("b_e2_sb", [H, 1])
        b_n1_sb = sb("b_n1_sb", [H, 1])
        b_n2_sb = sb("b_n2_sb", [H, 1])
        b_out_sb = sb("b_out_sb", [N, F])
        ones = sb("ones", [PARTS, H], BF16)
        x_uv = sb("x_uv", [F, N])
        x_out = sb("x_out", [F, N])
        x_nat = sb("x_nat", [N, F])
        x_bias = sb("x_bias", [N, F])
        uv_next = sb("uv_next", [H, 2, N])
        uv = sb("uv", [H, 2, N])
        y_ring = sb("y_ring", [H, Y_RING, TJ, N])
        e_ring = sb("e_ring", [H, 2, TJ, N])
        adj_blk = sb("adj_blk", [SPREAD, N])
        adj_rest = sb("adj_rest", [SPREAD, N])
        adj_parts = sb("adj_parts", [SPREAD, PARTS, N], BF16)
        adj_rows = sb("adj_rows", [PARTS, SPREAD * N], BF16)
        adj_wide = sb("adj_wide", [H, N - SPREAD, N])
        agg = sb("agg", [H, N])
        agg_full = sb("agg_full", [H, N])
        node1 = sb("node1", [H, N])
        node2 = sb("node2", [H, N])
        res = sb("res", [N, F])
        y_out = sb("y_out", [N, F])
        dev = sb("dev", [N, F])
        total = sb("total", [N, 1])
        mean = sb("mean", [N, 1])
        squares = sb("squares", [N, 1])
        var4 = sb("var4", [N, 1])
        std2 = sb("std2", [N, 1])
        inv2 = sb("inv2", [N, 1])
        std = sb("std", [N, 1])
        rstd = sb("rstd", [N, 1])
        root_in = sb("root_in", [N, 1])

        zs_ps = ps("zs_ps", [H, TJ * N])
        zc_ps = ps("zc_ps", [H, 2, TJ * N])
        a_ps = ps("a_ps", [H, BANK])
        once_ps = ps("once_ps", [H, BANK])
        node_ps = once_ps[:, 0:N]
        uv_ps = once_ps[:, N:3 * N]

        weights_in = sem("weights_in")
        ones_set = sem("ones_set")
        u_bias_set = sem("u_bias_set")
        root_in_set = sem("root_in_set")
        x_uv_in = sem("x_uv_in")
        x_out_in = sem("x_out_in")
        x_nat_in = sem("x_nat_in")
        adj_in = sem("adj_in")
        cut_step = sem("cut_step")
        rows_in = [sem("rows_in_0"), sem("rows_in_1")]
        low_in = [sem(f"low_in_{q}") for q in range(CHUNKS)]
        wide_in = [sem(f"wide_in_{q}") for q in range(CHUNKS)]
        uv_done = sem("uv_done")
        uv_saved = sem("uv_saved")
        uv_taken = sem("uv_taken")
        y_sum = sem("y_sum")
        y_ready = sem("y_ready")
        y_ready_dve = sem("y_ready_dve")
        z_ready = sem("z_ready")
        e_ready = sem("e_ready")
        a_ready = sem("a_ready")
        spread_agg = sem("spread_agg")
        copied_agg = sem("copied_agg")
        agg_saved = sem("agg_saved")
        node_mm = sem("node_mm")
        node_act = sem("node_act")
        res_bias = sem("res_bias")
        norm_step = sem("norm_step")
        root_done = sem("root_done")
        y_out_free = sem("y_out_free")

        NORM = 9
        ROOT_AT = 5
        WEIGHTS = 12

        def first_node(t):
            return t // 2 * TJ + (SPREAD if t % 2 else 0)

        block = ctx.enter_context(nc.Block())

        def batches(eng, body):
            body(0, first=True)
            with eng.Fori(1, B - 1) as b:
                body(b)
            body(B - 1, last=True)

        @block.sync
        def _(sp):
            sp.dma_start(x_uv[:], x_t[:, 0, :]).then_inc(x_uv_in, DMA)
            sp.dma_start(adj_blk[:], adj_t[0, 0:SPREAD]).then_inc(adj_in, DMA)
            for dst, src in (
                (w_u, w_e1[0:F]), (w_v, w_e1[F:2 * F]), (w_e2_sb, w_e2), (w_n1_sb, w_n1),
                (w_n2_sb, w_n2), (w_out_x, w_out[0:F]), (w_out_h, w_out[F:F + H]),
                (b_uv[:, 0:1], b_e1), (b_e2_sb, b_e2), (b_n1_sb, b_n1), (b_n2_sb, b_n2),
                (b_out_sb, b_out.partition_broadcast(N)),
            ):
                sp.dma_start(dst if isinstance(dst, bass.AP) else dst[:], src).then_inc(weights_in, DMA)

            def rows(b, half):
                sp.wait_ge(cut_step, 4 * b + 4)
                for part in range(PARTS):
                    dst = adj_rows[part:part + 1, half * ROWS * N:(half + 1) * ROWS * N]
                    sp.dma_start(dst.rearrange("p (j i) -> p j i", i=N),
                                 adj_parts[half * ROWS:(half + 1) * ROWS, part, :]
                                 ).then_inc(rows_in[half], DMA)

            def store(b):
                sp.wait_ge(norm_step, NORM * b + NORM)
                sp.dma_start(out[b], y_out[:]).then_inc(y_out_free, DMA)

            def copied(b, q):
                rows_q = slice(q * CHUNK, (q + 1) * CHUNK)
                src = adj_t[b, SPREAD + q * CHUNK:SPREAD + (q + 1) * CHUNK, :].rearrange("j i -> (j i)")
                low = adj_wide[0:H // 2, rows_q, :].rearrange("p j i -> p (j i)")
                high = adj_wide[H // 2:H, rows_q, :].rearrange("p j i -> p (j i)")
                sp.dma_start(low, src.partition_broadcast(H // 2)).then_inc(low_in[q], DMA)
                sp.wait_ge(low_in[q], DMA * (b + 1))
                sp.dma_start(high, low).then_inc(wide_in[q], DMA)

            rows(0, 0)
            rows(0, 1)
            for q in range(CHUNKS):
                copied(0, q)

            def body(b, first=False, last=False):
                def next_copied(b, q):
                    sp.wait_ge(copied_agg, TILES * b + 2 * (q + 1) * CHUNK // TJ)
                    copied(b + 1, q)

                if not last:
                    sp.wait_ge(uv_done, b + 1)
                    sp.dma_start(x_uv[:], x_t[:, b + 1, :]).then_inc(x_uv_in, DMA)
                    sp.wait_ge(cut_step, 4 * b + 4)
                    sp.dma_start(adj_blk[:], adj_t[b + 1, 0:SPREAD]).then_inc(adj_in, DMA)
                if not first:
                    next_copied(b - 1, CHUNKS - 1)
                if not last:
                    next_copied(b, 0)
                    next_copied(b, 1)
                    sp.wait_ge(a_ready, TILES * b + PAIRS)
                    rows(b + 1, 0)
                    next_copied(b, 2)
                if not first:
                    sp.wait_ge(node_mm, 3 * b)
                    sp.wait_ge(res_bias, b)
                sp.dma_start(x_out[:], x_t[:, b, :]).then_inc(x_out_in, DMA)
                sp.dma_start(x_nat[:], x[b]).then_inc(x_nat_in, DMA)
                if not last:
                    sp.wait_ge(a_ready, TILES * b + TILES)
                    rows(b + 1, 1)
                if not first:
                    store(b - 1)

            batches(sp, body)
            store(B - 1)
            sp.wait_ge(y_out_free, DMA * (B + 1))

        @block.gpsimd
        def _(pool):
            nc.gpsimd.memset(ones[:], 1.0).then_inc(ones_set, 1)
            nc.gpsimd.memset(b_uv[:, 1:2], 0.0).then_inc(u_bias_set, 1)
            pool.wait_ge(u_bias_set, 1)
            pool.wait_ge(weights_in, DMA * WEIGHTS)

            def residual(b):
                pool.wait_ge(x_nat_in, DMA * b + DMA)
                pool.wait_ge(agg_saved, b + 1)
                nc.gpsimd.tensor_tensor(x_bias[:], x_nat[:], b_out_sb[:], ALU.add).then_inc(res_bias, 1)

            def body(b, first=False, last=False):
                pool.wait_ge(uv_saved, b + 1)
                if not first:
                    pool.wait_ge(y_sum, TILES * b)
                nc.gpsimd.tensor_tensor(uv[:], uv_next[:], b_uv[:].unsqueeze(2).broadcast_to([H, 2, N]),
                                        ALU.add).then_inc(uv_taken, 1)
                pool.wait_ge(uv_taken, b + 1)
                for t in range(TILES):
                    if not (first and t < Y_RING):
                        pool.wait_ge(z_ready, TILES * b + t - Y_RING + 1)
                    v = uv[:, 0, :].unsqueeze(1).broadcast_to([H, TJ, N])
                    j = first_node(t)
                    u = uv[:, 1, j:j + TJ].unsqueeze(2).broadcast_to([H, TJ, N])
                    nc.gpsimd.tensor_tensor(y_ring[:, t % Y_RING], v, u, ALU.add).then_inc(y_sum, 1)
                    if t == POOL_RESIDUAL and not first:
                        residual(b - 1)

            batches(pool, body)
            residual(B - 1)

        @block.scalar
        def _(act):
            act.wait_ge(root_in_set, 1)
            nc.scalar.activation(root_in[:], root_in[:], ACT.Sqrt)
            act.wait_ge(weights_in, DMA * WEIGHTS)

            def relu_y(b, t):
                if t % TILES in Y_BY_DVE:
                    return
                slot = y_ring[:, t % Y_RING]
                act.wait_ge(y_sum, TILES * b + t + 1)
                nc.scalar.activation(slot, slot, ACT.Relu).then_inc(y_ready, 1)

            def relu_e(b, t, first):
                pair = PAIRS * b + t // 2
                act.wait_ge(z_ready, TILES * b + t + 1)
                if t % 2:
                    src = dst = zc_ps[:, t // 2 % 2]
                else:
                    src, dst = zs_ps[:], e_ring[:, t // 2 % 2].rearrange("p j i -> p (j i)")
                    if not (first and t < 4):
                        act.wait_ge(spread_agg, 2 * (pair - 1))
                nc.scalar.activation(dst, src, ACT.Relu, bias=b_e2_sb[:]).then_inc(e_ready, 1)

            def node_relu(b, layer):
                dst, bias = ((node1, b_n1_sb), (node2, b_n2_sb))[layer]
                act.wait_ge(node_mm, 3 * b + layer + 1)
                nc.scalar.activation(dst[:], node_ps, ACT.Relu, bias=bias[:]).then_inc(node_act, 1)

            def root(b):
                act.wait_ge(norm_step, NORM * b + ROOT_AT)
                nc.scalar.activation(std2[:], var4[:], ACT.Sqrt).then_inc(root_done, 1)

            def body(b, first=False, last=False):
                for t in range(TILES):
                    relu_e(b, t, first)
                    if not (last and t + Y_AHEAD >= TILES):
                        relu_y(b, t + Y_AHEAD)
                    if not first:
                        if t == ACT_NODE1:
                            node_relu(b - 1, 0)
                        if t == ACT_NODE2:
                            node_relu(b - 1, 1)
                        if t == ACT_ROOT:
                            root(b - 1)

            for t in range(Y_AHEAD):
                relu_y(0, t)
            batches(act, body)
            node_relu(B - 1, 0)
            node_relu(B - 1, 1)
            root(B - 1)

        @block.vector
        def _(dve):
            nc.vector.memset(root_in[:], 1.0).then_inc(root_in_set, 1)
            nc.vector.memset(y_out[:], 0.0).then_inc(y_out_free, DMA)
            dve.wait_ge(weights_in, DMA * WEIGHTS)

            def cut(b, step, whole=False):
                hi, mid, lo = (adj_parts[:, part, :] for part in range(PARTS))
                if step == 0:
                    dve.wait_ge(adj_in, DMA * b + DMA)
                    if not whole:
                        for half in range(2):
                            dve.wait_ge(rows_in[half], DMA * PARTS * b)
                    ins = nc.vector.tensor_copy(hi, adj_blk[:])
                if step == 1:
                    dve.wait_ge(cut_step, 4 * b + 1)
                    ins = nc.vector.tensor_tensor(adj_rest[:], adj_blk[:], hi, ALU.subtract)
                if step == 2:
                    dve.wait_ge(cut_step, 4 * b + 2)
                    ins = nc.vector.tensor_copy(mid, adj_rest[:])
                if step == 3:
                    dve.wait_ge(cut_step, 4 * b + 3)
                    ins = nc.vector.tensor_tensor(lo, adj_rest[:], mid, ALU.subtract)
                ins.then_inc(cut_step, 1)

            def save_uv(b, first=False):
                dve.wait_ge(uv_done, b + 1)
                if not first:
                    dve.wait_ge(uv_taken, b)
                nc.vector.tensor_copy(uv_next[:].rearrange("p s i -> p (s i)"), uv_ps
                                      ).then_inc(uv_saved, 1)

            def aggregate(b, t, half, first):
                dve.wait_ge(e_ready, TILES * b + t + 1)
                if t == 0 and half == 0 and not first:
                    dve.wait_ge(agg_saved, b)
                pair = PAIRS * b + t // 2
                for k in range(HALF):
                    n = half * HALF + k
                    j = first_node(t) + n
                    if t % 2:
                        if k == 0:
                            q, at = divmod(j - SPREAD, CHUNK)
                            if at == 0:
                                dve.wait_ge(wide_in[q], DMA * (b + 1))
                        e = zc_ps[:, t // 2 % 2, n * N:(n + 1) * N]
                        adj = adj_wide[:, j - SPREAD, :]
                    else:
                        if k == 0:
                            dve.wait_ge(a_ready, 2 * pair + half + 1)
                        e = e_ring[:, t // 2 % 2, n, :]
                        adj = a_ps[:, k * N:(k + 1) * N]
                    ins = nc.vector.tensor_tensor_reduce(e, e, adj, 1.0, 0.0, ALU.mult, ALU.add,
                                                         agg[:, j:j + 1])
                ins.then_inc(copied_agg if t % 2 else spread_agg, 1)

            def save_agg(b, first):
                dve.wait_ge(spread_agg, TILES * (b + 1))
                dve.wait_ge(copied_agg, TILES * (b + 1))
                if not first:
                    dve.wait_ge(node_mm, 3 * b)
                nc.vector.tensor_copy(agg_full[:], agg[:]).then_inc(agg_saved, 1)

            def relu_y(b, t):
                slot = y_ring[:, t % Y_RING]
                dve.wait_ge(y_sum, TILES * b + t + 1)
                nc.vector.tensor_scalar(slot, slot, 0.0, None, ALU.max).then_inc(y_ready_dve, 1)

            def norm(b, step):
                if step == 0:
                    dve.wait_ge(node_mm, 3 * b + 3)
                    dve.wait_ge(res_bias, b + 1)
                    ins = nc.vector.scalar_tensor_tensor(out=res[:], in0=node_ps[:, 0:F], scalar=0.0,
                                                         in1=x_bias[:], op0=ALU.add, op1=ALU.add,
                                                         accum_out=total[:])
                elif step == ROOT_AT:
                    dve.wait_ge(root_done, b + 1)
                else:
                    dve.wait_ge(norm_step, NORM * b + step)
                if step == 1:
                    ins = nc.vector.tensor_scalar(mean[:], total[:], 1.0 / F, None, ALU.mult)
                if step == 2:
                    ins = nc.vector.tensor_scalar(dev[:], res[:], mean[:], None, ALU.subtract)
                if step == 3:
                    ins = nc.vector.scalar_tensor_tensor(out=res[:], in0=dev[:], scalar=1.0, in1=dev[:],
                                                         op0=ALU.mult, op1=ALU.mult, accum_out=squares[:])
                if step == 4:
                    ins = nc.vector.tensor_scalar(var4[:], squares[:], 0.25 / F, 0.25 * LN_EPS, ALU.mult,
                                                  ALU.add)
                if step == 5:
                    ins = nc.vector.reciprocal(inv2[:], std2[:])
                if step == 6:
                    ins = nc.vector.scalar_tensor_tensor(out=std[:], in0=var4[:], scalar=inv2[:],
                                                         in1=std2[:], op0=ALU.mult, op1=ALU.add)
                if step == 7:
                    ins = nc.vector.reciprocal(rstd[:], std[:])
                if step == 8:
                    dve.wait_ge(y_out_free, DMA * (b + 1))
                    ins = nc.vector.tensor_scalar(y_out[:], dev[:], rstd[:], None, ALU.mult)
                ins.then_inc(norm_step, 1)

            def body(b, first=False, last=False):
                for pair in range(PAIRS):
                    for n, (tile, half) in enumerate(((0, 0), (1, 0), (0, 1), (1, 1))):
                        at = 4 * pair + n
                        aggregate(b, 2 * pair + tile, half, first)
                        if at in DVE_RELU:
                            relu_y(b, DVE_RELU[at])
                        if at in DVE_CUT and not last:
                            cut(b + 1, DVE_CUT.index(at))
                        if at == DVE_UV and not last:
                            save_uv(b + 1)
                        if at in DVE_NORM and not first:
                            norm(b - 1, DVE_NORM.index(at))
                save_agg(b, first)

            for step in range(4):
                cut(0, step, whole=True)
            save_uv(0, first=True)
            batches(dve, body)
            for step in range(NORM):
                norm(B - 1, step)

        @block.tensor
        def _(pe):
            pe.wait_ge(weights_in, DMA * WEIGHTS)
            pe.wait_ge(ones_set, 1)

            def uv_products(b):
                pe.wait_ge(x_uv_in, DMA * b + DMA)
                if not (isinstance(b, int) and b == 0):
                    pe.wait_ge(uv_saved, b)
                nc.tensor.matmul(uv_ps[:, 0:N], w_v[:], x_uv[:], start=True, stop=True)
                nc.tensor.matmul(uv_ps[:, N:2 * N], w_u[:], x_uv[:], start=True, stop=True
                                 ).then_inc(uv_done, 1)

            def z_half(b, t, half, first=False):
                if half == 0:
                    if t % TILES in Y_BY_DVE:
                        pe.wait_ge(y_ready_dve, len(Y_BY_DVE) * b + Y_BY_DVE.index(t) + 1)
                    else:
                        before = sum(t >= d for d in Y_BY_DVE)
                        pe.wait_ge(y_ready, Y_BY_ACT * b + t - before + 1)
                    pair = PAIRS * b + t // 2
                    if t % 2 == 0 and not (first and t < 2):
                        pe.wait_ge(e_ready, TILES * b + t - 1)
                    if t % 2 == 1 and not (first and t < 4):
                        pe.wait_ge(copied_agg, 2 * (pair - 1))
                z = zc_ps[:, t // 2 % 2] if t % 2 else zs_ps[:]
                y = y_ring[:, t % Y_RING, half * HALF:(half + 1) * HALF, :].rearrange("p j i -> p (j i)")
                mm = nc.tensor.matmul(z[:, half * BANK:(half + 1) * BANK], w_e2_sb[:], y,
                                      start=True, stop=True)
                if half == 1:
                    mm.then_inc(z_ready, 1)

            def spread(b, pair, half, first):
                if pair % (PAIRS // 2) == 0 and half == 0:
                    pe.wait_ge(rows_in[2 * pair // PAIRS], DMA * PARTS * (b + 1))
                if not (first and pair == 0 and half == 0):
                    pe.wait_ge(spread_agg, 2 * (PAIRS * b + pair) + half)
                at = (pair * TJ + half * HALF) * N
                nc.tensor.matmul(a_ps[:], ones[:], adj_rows[:, at:at + BANK], start=True,
                                 stop=True).then_inc(a_ready, 1)

            def node_product(b, layer, last=False):
                if layer == 0:
                    pe.wait_ge(agg_saved, b + 1)
                    if not last:
                        pe.wait_ge(uv_saved, b + 3)
                    nc.tensor.matmul(node_ps, w_n1_sb[:], agg_full[:], start=True, stop=True
                                     ).then_inc(node_mm, 1)
                if layer == 1:
                    pe.wait_ge(node_act, 2 * b + 1)
                    nc.tensor.matmul(node_ps, w_n2_sb[:], node1[:], start=True, stop=True
                                     ).then_inc(node_mm, 1)
                if layer == 2:
                    pe.wait_ge(node_act, 2 * b + 2)
                    pe.wait_ge(x_out_in, DMA * b + DMA)
                    nc.tensor.matmul(node_ps[:, 0:F], x_out[:], w_out_x[:], start=True, stop=False)
                    nc.tensor.matmul(node_ps[:, 0:F], node2[:], w_out_h[:], start=False, stop=True
                                     ).then_inc(node_mm, 1)

            def body(b, first=False, last=False):
                for pair in range(PAIRS):
                    ahead = not (last and pair == PAIRS - 1)
                    t = 2 * (pair + 1)
                    if ahead:
                        z_half(b, t, 0)
                    spread(b, pair, 0, first)
                    if ahead:
                        z_half(b, t, 1)
                        z_half(b, t + 1, 0, first)
                    spread(b, pair, 1, first)
                    if ahead:
                        z_half(b, t + 1, 1)
                    if pair == PE_UV and not last:
                        if not first:
                            pe.wait_ge(agg_saved, b)
                        uv_products(b + 1)
                    if pair in PE_NODE and not first:
                        node_product(b - 1, PE_NODE.index(pair), last)

            uv_products(0)
            for t in range(2):
                for half in range(2):
                    z_half(0, t, half, first=True)
            batches(pe, body)
            for layer in range(3):
                node_product(B - 1, layer, last=True)


def kernel(x, adj, L0_gnn_W_e1, L0_gnn_b_e1, L0_gnn_W_e2, L0_gnn_b_e2, L0_gnn_W_n1, L0_gnn_b_n1,
           L0_gnn_W_n2, L0_gnn_b_n2, L0_gnn_W_out, L0_gnn_b_out):
    import numpy as np
    import concourse.bacc as bacc
    from concourse.bass_utils import run_bass_kernel_spmd

    def laid(a):
        return np.ascontiguousarray(a)

    def column(a):
        return laid(np.asarray(a).reshape(-1, 1))

    x, adj = np.asarray(x), np.asarray(adj)
    arrays = {
        "x": laid(x),
        "x_t": laid(x.transpose(2, 0, 1)),
        "adj_t": laid(adj.transpose(0, 2, 1)),
        "w_e1": laid(L0_gnn_W_e1), "b_e1": column(L0_gnn_b_e1),
        "w_e2": laid(L0_gnn_W_e2), "b_e2": column(L0_gnn_b_e2),
        "w_n1": laid(L0_gnn_W_n1), "b_n1": column(L0_gnn_b_n1),
        "w_n2": laid(L0_gnn_W_n2), "b_n2": column(L0_gnn_b_n2),
        "w_out": laid(L0_gnn_W_out), "b_out": laid(L0_gnn_b_out),
    }
    nc = bacc.Bacc("TRN2", target_bir_lowering=False, num_devices=1)
    args = [nc.dram_tensor(name, a.shape, mybir.dt.from_np(a.dtype), kind="ExternalInput").ap()
            for name, a in arrays.items()]
    out = nc.dram_tensor("out", x.shape, F32, kind="ExternalOutput").ap()
    build_gnn(nc, *args, out)
    result = run_bass_kernel_spmd(nc, [arrays], core_ids=[0])
    return result.results[0]["out"]
```

```python
from contextlib import ExitStack

import concourse.bass as bass
from concourse import mybir

ALU = mybir.AluOpType
ACT = mybir.ActivationFunctionType
F32 = mybir.dt.float32
BF16 = mybir.dt.bfloat16

TJ = 8
BANK = 512
Y_RING = 4
Y_AHEAD = 2
PARTS = 3
DMA = 16
LN_EPS = 1e-5

PE_UV, PE_NODE = 1, (2, 3, 4)
ACT_NODE1, ACT_NODE2, ACT_ROOT = 7, 9, 13
DVE_UV = 7
DVE_CUT = (8, 10, 12, 14)
DVE_NORM = (18, 20, 21, 22, 23, 28, 29, 30, 31)
DVE_RELU = {17: 6}
POOL_RESIDUAL = 4


def build_gnn(nc, x, x_t, adj_t, w_e1, b_e1, w_e2, b_e2, w_n1, b_n1, w_n2, b_n2, w_out, b_out, out):
    B, N, F = x.shape
    H = w_e2.shape[0]
    TILES = N // TJ
    PAIRS = TILES // 2
    HALF = BANK // N
    QUARTER = N // 4
    SPREAD = QUARTER
    ROWS = SPREAD // 2
    CHUNKS = PAIRS // 2
    Y_BY_DVE = sorted(DVE_RELU.values())
    assert N == 128 and H == 128 and 2 * F == w_e1.shape[0] and TJ == 2 * HALF
    assert PAIRS % Y_RING == 0 and PAIRS % 4 == 0

    with ExitStack() as ctx:
        def sb(name, shape, dt=F32):
            return ctx.enter_context(nc.sbuf_tensor(name, shape, dt))

        def ps(name, shape):
            return ctx.enter_context(nc.psum_tensor(name, shape, F32))

        def sem(name):
            return ctx.enter_context(nc.semaphore(name))

        w_u = sb("w_u", [F, H])
        w_v = sb("w_v", [F, H])
        w_e2_sb = sb("w_e2_sb", [H, H])
        w_n1_sb = sb("w_n1_sb", [H, H])
        w_n2_sb = sb("w_n2_sb", [H, H])
        w_out_x = sb("w_out_x", [F, F])
        w_out_h = sb("w_out_h", [H, F])
        b_uv = sb("b_uv", [H, 2])
        b_e2_sb = sb("b_e2_sb", [H, 1])
        b_n1_sb = sb("b_n1_sb", [H, 1])
        b_n2_sb = sb("b_n2_sb", [H, 1])
        b_out_sb = sb("b_out_sb", [N, F])
        ones = sb("ones", [PARTS, H], BF16)
        x_uv = sb("x_uv", [F, N])
        x_out = sb("x_out", [F, N])
        x_nat = sb("x_nat", [N, F])
        x_bias = sb("x_bias", [N, F])
        uv_next = sb("uv_next", [H, 2, N])
        uv = sb("uv", [H, 2, N])
        y_ring = sb("y_ring", [H, Y_RING, 2 * TJ, N])
        e_ring = sb("e_ring", [H, 2, TJ, N])
        adj_blk = sb("adj_blk", [SPREAD, N])
        adj_rest = sb("adj_rest", [SPREAD, N])
        adj_parts = sb("adj_parts", [SPREAD, PARTS, N], BF16)
        adj_rows = sb("adj_rows", [PARTS, SPREAD * N], BF16)
        adj_wide = sb("adj_wide", [H, CHUNKS, 3, TJ, N])
        agg = sb("agg", [H, N])
        agg_full = sb("agg_full", [H, N])
        node1 = sb("node1", [H, N])
        node2 = sb("node2", [H, N])
        res = sb("res", [N, F])
        y_out = sb("y_out", [N, F])
        dev = sb("dev", [N, F])
        total = sb("total", [N, 1])
        mean = sb("mean", [N, 1])
        squares = sb("squares", [N, 1])
        var4 = sb("var4", [N, 1])
        std2 = sb("std2", [N, 1])
        inv2 = sb("inv2", [N, 1])
        std = sb("std", [N, 1])
        rstd = sb("rstd", [N, 1])
        root_in = sb("root_in", [N, 1])

        zs_ps = ps("zs_ps", [H, TJ * N])
        zc_ps = ps("zc_ps", [H, 2, TJ * N])
        a_ps = ps("a_ps", [H, BANK])
        once_ps = ps("once_ps", [H, BANK])
        node_ps = once_ps[:, 0:N]
        uv_ps = once_ps[:, N:3 * N]

        uv_weights_in = sem("uv_weights_in")
        edge_weights_in = sem("edge_weights_in")
        node_weights_in = sem("node_weights_in")
        ones_set = sem("ones_set")
        u_bias_set = sem("u_bias_set")
        root_in_set = sem("root_in_set")
        x_uv_in = sem("x_uv_in")
        x_out_in = sem("x_out_in")
        x_nat_in = sem("x_nat_in")
        adj_in = sem("adj_in")
        cut_step = sem("cut_step")
        rows_in = [sem("rows_in_0"), sem("rows_in_1")]
        low_in = [sem(f"low_in_{q}") for q in range(CHUNKS)]
        wide_in = [sem(f"wide_in_{q}") for q in range(CHUNKS)]
        uv_done = sem("uv_done")
        uv_saved = sem("uv_saved")
        uv_taken = sem("uv_taken")
        y_sum = sem("y_sum")
        y_ready = sem("y_ready")
        y_ready_dve = sem("y_ready_dve")
        z_ready = sem("z_ready")
        e_ready = sem("e_ready")
        a_ready = sem("a_ready")
        first_agg = sem("first_agg")
        second_agg = sem("second_agg")
        agg_saved = sem("agg_saved")
        node_mm = sem("node_mm")
        node_act = sem("node_act")
        res_bias = sem("res_bias")
        norm_step = sem("norm_step")
        root_done = sem("root_done")
        y_out_free = sem("y_out_free")

        NORM = 9
        ROOT_AT = 5

        def first_node(t):
            second, pair = t % 2, t // 2
            return (2 * second + pair % 2) * QUARTER + pair // 2 * TJ

        uv_weights = ((w_v[:], w_e1[F:2 * F]), (w_u[:], w_e1[0:F]), (b_uv[:, 0:1], b_e1))
        edge_weights = ((w_e2_sb[:], w_e2), (b_e2_sb[:], b_e2))
        node_weights = ((w_n1_sb[:], w_n1), (w_n2_sb[:], w_n2), (w_out_x[:], w_out[0:F]),
                        (w_out_h[:], w_out[F:F + H]), (b_n1_sb[:], b_n1), (b_n2_sb[:], b_n2),
                        (b_out_sb[:], b_out.partition_broadcast(N)))

        block = ctx.enter_context(nc.Block())

        def batches(eng, body):
            body(0, first=True)
            with eng.Fori(1, B - 1) as b:
                body(b)
            body(B - 1, last=True)

        @block.sync
        def _(sp):
            sp.dma_start(x_uv[:], x_t[:, 0, :]).then_inc(x_uv_in, DMA)
            for dst, src in uv_weights:
                sp.dma_start(dst, src).then_inc(uv_weights_in, DMA)

            def rows(b, half):
                sp.wait_ge(cut_step, 4 * b + 4)
                for part in range(PARTS):
                    dst = adj_rows[part:part + 1, half * ROWS * N:(half + 1) * ROWS * N]
                    sp.dma_start(dst.rearrange("p (j i) -> p j i", i=N),
                                 adj_parts[half * ROWS:(half + 1) * ROWS, part, :]
                                 ).then_inc(rows_in[half], DMA)

            def load_x_uv(b):
                sp.wait_ge(uv_done, b)
                sp.dma_start(x_uv[:], x_t[:, b, :]).then_inc(x_uv_in, DMA)

            def store(b):
                sp.wait_ge(norm_step, NORM * b + NORM)
                sp.dma_start(out[b], y_out[:]).then_inc(y_out_free, DMA)

            def copied_low(b, q):
                src = adj_t[b, SPREAD:N, :].rearrange("(s q j) i -> q s (j i)", s=3, j=TJ)[q]
                low = adj_wide[0:H // 2, q].rearrange("p s j i -> p s (j i)")
                sp.dma_start(low, src.partition_broadcast(H // 2)).then_inc(low_in[q], DMA)

            def copied_high(b, q):
                sp.wait_ge(low_in[q], DMA * (b + 1))
                sp.dma_start(adj_wide[H // 2:H, q], adj_wide[0:H // 2, q]).then_inc(wide_in[q], DMA)

            copied_low(0, 0)
            rows(0, 0)
            copied_high(0, 0)
            load_x_uv(1)
            rows(0, 1)
            copied_low(0, 1)
            for dst, src in node_weights[3:]:
                sp.dma_start(dst, src).then_inc(node_weights_in, DMA)
            for q in range(1, CHUNKS):
                if q + 1 < CHUNKS:
                    copied_low(0, q + 1)
                copied_high(0, q)

            def body(b, first=False, last=False, next_last=False):
                def next_low(b, q):
                    sp.wait_ge(second_agg, TILES * b + 4 * (q + 1))
                    sp.wait_ge(first_agg, TILES * b + 4 * (q + 1))
                    copied_low(b + 1, q)

                if not last:
                    sp.wait_ge(cut_step, 4 * b + 4)
                    sp.dma_start(adj_blk[:], adj_t[b + 1, 0:SPREAD]).then_inc(adj_in, DMA)
                if not first:
                    next_low(b - 1, CHUNKS - 1)
                    copied_high(b, CHUNKS - 1)
                if not last:
                    next_low(b, 0)
                    sp.wait_ge(a_ready, PAIRS * b + PAIRS // 2)
                    rows(b + 1, 0)
                    copied_high(b + 1, 0)
                    next_low(b, 1)
                if not first:
                    sp.wait_ge(node_mm, 3 * b)
                    sp.wait_ge(res_bias, b)
                sp.dma_start(x_out[:], x_t[:, b, :]).then_inc(x_out_in, DMA)
                sp.dma_start(x_nat[:], x[b]).then_inc(x_nat_in, DMA)
                if not last:
                    copied_high(b + 1, 1)
                    next_low(b, 2)
                    if not next_last:
                        load_x_uv(b + 2)
                    sp.wait_ge(a_ready, PAIRS * b + PAIRS)
                    rows(b + 1, 1)
                    copied_high(b + 1, 2)
                if not first:
                    store(b - 1)

            body(0, first=True)
            with sp.Fori(1, B - 2) as b:
                body(b)
            body(B - 2, next_last=True)
            body(B - 1, last=True)
            store(B - 1)
            sp.wait_ge(y_out_free, DMA * (B + 1))

        @block.gpsimd
        def _(pool):
            nc.gpsimd.memset(ones[:], 1.0).then_inc(ones_set, 1)
            nc.gpsimd.memset(b_uv[:, 1:2], 0.0).then_inc(u_bias_set, 1)
            pool.wait_ge(u_bias_set, 1)
            pool.wait_ge(uv_weights_in, DMA * len(uv_weights))

            def residual(b):
                pool.wait_ge(node_weights_in, DMA * len(node_weights))
                pool.wait_ge(x_nat_in, DMA * b + DMA)
                pool.wait_ge(agg_saved, b + 1)
                nc.gpsimd.tensor_tensor(x_bias[:], x_nat[:], b_out_sb[:], ALU.add).then_inc(res_bias, 1)

            def body(b, first=False, last=False):
                pool.wait_ge(uv_saved, b + 1)
                if not first:
                    pool.wait_ge(y_sum, PAIRS * b + 1)
                nc.gpsimd.tensor_tensor(uv[:], uv_next[:], b_uv[:].unsqueeze(2).broadcast_to([H, 2, N]),
                                        ALU.add).then_inc(uv_taken, 1)
                pool.wait_ge(uv_taken, b + 1)
                for pair in range(PAIRS):
                    if not (first and pair < Y_RING):
                        pool.wait_ge(z_ready, TILES * b + 2 * (pair - Y_RING + 1))
                    at = first_node(2 * pair)
                    for tiles in ((0,), (1,)) if first and pair == 0 else ((0, 1),):
                        n = len(tiles)
                        lo, hi = tiles[0], tiles[-1] + 1
                        v = uv[:, 0, :].unsqueeze(1).broadcast_to([H, n * TJ, N])
                        u = uv[:, 1, :].rearrange("p (s j) -> p s j", s=2)[:, lo:hi, at:at + TJ]
                        y = y_ring[:, pair % Y_RING, lo * TJ:hi * TJ, :]
                        nc.gpsimd.tensor_tensor(y.rearrange("p (s j) i -> p s j i", s=n),
                                                v.rearrange("p (s j) i -> p s j i", s=n),
                                                u.unsqueeze(3).broadcast_to([H, n, TJ, N]),
                                                ALU.add).then_inc(y_sum, 1)
                    if pair == POOL_RESIDUAL and not first:
                        residual(b - 1)

            batches(pool, body)
            residual(B - 1)

        @block.scalar
        def _(act):
            act.dma_start(adj_blk[:], adj_t[0, 0:SPREAD]).then_inc(adj_in, DMA)
            for dst, src in edge_weights:
                act.dma_start(dst, src).then_inc(edge_weights_in, DMA)
            act.wait_ge(root_in_set, 1)
            nc.scalar.activation(root_in[:], root_in[:], ACT.Sqrt)
            for dst, src in node_weights[:3]:
                act.dma_start(dst, src).then_inc(node_weights_in, DMA)
            act.wait_ge(edge_weights_in, DMA * len(edge_weights))

            def relu_y(b, pair):
                tiles = 1 if pair % PAIRS in Y_BY_DVE else 2
                slot = y_ring[:, pair % Y_RING, 0:tiles * TJ, :]
                act.wait_ge(y_sum, PAIRS * b + pair + 2)
                nc.scalar.activation(slot, slot, ACT.Relu).then_inc(y_ready, 1)

            def relu_first_y(tile):
                slot = y_ring[:, 0, tile * TJ:(tile + 1) * TJ, :]
                act.wait_ge(y_sum, tile + 1)
                nc.scalar.activation(slot, slot, ACT.Relu).then_inc(y_ready, 1)

            def relu_e(b, t, first):
                pair = PAIRS * b + t // 2
                act.wait_ge(z_ready, TILES * b + t + 1)
                if t % 2:
                    src = dst = zc_ps[:, t // 2 % 2]
                else:
                    src, dst = zs_ps[:], e_ring[:, t // 2 % 2].rearrange("p j i -> p (j i)")
                    if not (first and t < 4):
                        act.wait_ge(first_agg, 2 * (pair - 1))
                nc.scalar.activation(dst, src, ACT.Relu, bias=b_e2_sb[:]).then_inc(e_ready, 1)

            def node_relu(b, layer):
                dst, bias = ((node1, b_n1_sb), (node2, b_n2_sb))[layer]
                act.wait_ge(node_weights_in, DMA * len(node_weights))
                act.wait_ge(node_mm, 3 * b + layer + 1)
                nc.scalar.activation(dst[:], node_ps, ACT.Relu, bias=bias[:]).then_inc(node_act, 1)

            def root(b):
                act.wait_ge(norm_step, NORM * b + ROOT_AT)
                nc.scalar.activation(std2[:], var4[:], ACT.Sqrt).then_inc(root_done, 1)

            def body(b, first=False, last=False):
                for t in range(TILES):
                    relu_e(b, t, first)
                    pair = t // 2 + Y_AHEAD
                    if t % 2 == 0 and not (last and pair >= PAIRS):
                        relu_y(b, pair)
                    if not first:
                        if t == ACT_NODE1:
                            node_relu(b - 1, 0)
                        if t == ACT_NODE2:
                            node_relu(b - 1, 1)
                        if t == ACT_ROOT:
                            root(b - 1)

            for tile in range(2):
                relu_first_y(tile)
            for pair in range(1, Y_AHEAD):
                relu_y(0, pair)
            batches(act, body)
            node_relu(B - 1, 0)
            node_relu(B - 1, 1)
            root(B - 1)

        @block.vector
        def _(dve):
            nc.vector.memset(root_in[:], 1.0).then_inc(root_in_set, 1)
            nc.vector.memset(y_out[:], 0.0).then_inc(y_out_free, DMA)

            def cut(b, step, whole=False):
                hi, mid, lo = (adj_parts[:, part, :] for part in range(PARTS))
                if step == 0:
                    dve.wait_ge(adj_in, DMA * b + DMA)
                    if not whole:
                        for half in range(2):
                            dve.wait_ge(rows_in[half], DMA * PARTS * b)
                    ins = nc.vector.tensor_copy(hi, adj_blk[:])
                if step == 1:
                    dve.wait_ge(cut_step, 4 * b + 1)
                    ins = nc.vector.tensor_tensor(adj_rest[:], adj_blk[:], hi, ALU.subtract)
                if step == 2:
                    dve.wait_ge(cut_step, 4 * b + 2)
                    ins = nc.vector.tensor_copy(mid, adj_rest[:])
                if step == 3:
                    dve.wait_ge(cut_step, 4 * b + 3)
                    ins = nc.vector.tensor_tensor(lo, adj_rest[:], mid, ALU.subtract)
                ins.then_inc(cut_step, 1)

            def save_uv(b, first=False):
                dve.wait_ge(uv_done, b + 1)
                if not first:
                    dve.wait_ge(uv_taken, b)
                nc.vector.tensor_copy(uv_next[:].rearrange("p s i -> p (s i)"), uv_ps
                                      ).then_inc(uv_saved, 1)

            def aggregate(b, t, half, first):
                dve.wait_ge(e_ready, TILES * b + t + 1)
                if t < 2 and half == 0 and not first:
                    dve.wait_ge(agg_saved, b)
                spread_tile = t % 4 == 0
                for k in range(HALF):
                    n = half * HALF + k
                    j = first_node(t) + n
                    if t % 2:
                        e = zc_ps[:, t // 2 % 2, n * N:(n + 1) * N]
                    else:
                        e = e_ring[:, t // 2 % 2, n, :]
                    if spread_tile:
                        if k == 0:
                            dve.wait_ge(a_ready, PAIRS * b + t // 2 + half + 1)
                        adj = a_ps[:, k * N:(k + 1) * N]
                    else:
                        if k == 0 and t % 4 == 1:
                            dve.wait_ge(wide_in[t // 4], DMA * (b + 1))
                        adj = adj_wide[:, t // 4, (1, 0, 2)[t % 4 - 1], n, :]
                    ins = nc.vector.tensor_tensor_reduce(e, e, adj, 1.0, 0.0, ALU.mult, ALU.add,
                                                         agg[:, j:j + 1])
                ins.then_inc(second_agg if t % 2 else first_agg, 1)

            def save_agg(b, first):
                dve.wait_ge(first_agg, TILES * (b + 1))
                dve.wait_ge(second_agg, TILES * (b + 1))
                if not first:
                    dve.wait_ge(node_mm, 3 * b)
                nc.vector.tensor_copy(agg_full[:], agg[:]).then_inc(agg_saved, 1)

            def relu_y(b, pair):
                slot = y_ring[:, pair % Y_RING, TJ:2 * TJ, :]
                dve.wait_ge(y_sum, PAIRS * b + pair + 2)
                nc.vector.tensor_scalar(slot, slot, 0.0, None, ALU.max).then_inc(y_ready_dve, 1)

            def norm(b, step):
                if step == 0:
                    dve.wait_ge(node_mm, 3 * b + 3)
                    dve.wait_ge(res_bias, b + 1)
                    ins = nc.vector.scalar_tensor_tensor(out=res[:], in0=node_ps[:, 0:F], scalar=0.0,
                                                         in1=x_bias[:], op0=ALU.add, op1=ALU.add,
                                                         accum_out=total[:])
                elif step == ROOT_AT:
                    dve.wait_ge(root_done, b + 1)
                else:
                    dve.wait_ge(norm_step, NORM * b + step)
                if step == 1:
                    ins = nc.vector.tensor_scalar(mean[:], total[:], 1.0 / F, None, ALU.mult)
                if step == 2:
                    ins = nc.vector.tensor_scalar(dev[:], res[:], mean[:], None, ALU.subtract)
                if step == 3:
                    ins = nc.vector.scalar_tensor_tensor(out=res[:], in0=dev[:], scalar=1.0, in1=dev[:],
                                                         op0=ALU.mult, op1=ALU.mult, accum_out=squares[:])
                if step == 4:
                    ins = nc.vector.tensor_scalar(var4[:], squares[:], 0.25 / F, 0.25 * LN_EPS, ALU.mult,
                                                  ALU.add)
                if step == 5:
                    ins = nc.vector.reciprocal(inv2[:], std2[:])
                if step == 6:
                    ins = nc.vector.scalar_tensor_tensor(out=std[:], in0=var4[:], scalar=inv2[:],
                                                         in1=std2[:], op0=ALU.mult, op1=ALU.add)
                if step == 7:
                    ins = nc.vector.reciprocal(rstd[:], std[:])
                if step == 8:
                    dve.wait_ge(y_out_free, DMA * (b + 1))
                    ins = nc.vector.tensor_scalar(y_out[:], dev[:], rstd[:], None, ALU.mult)
                ins.then_inc(norm_step, 1)

            def body(b, first=False, last=False):
                for pair in range(PAIRS):
                    for n, (tile, half) in enumerate(((0, 0), (1, 0), (1, 1), (0, 1))):
                        at = 4 * pair + n
                        aggregate(b, 2 * pair + tile, half, first)
                        if at in DVE_RELU:
                            relu_y(b, DVE_RELU[at])
                        if at in DVE_CUT and not last:
                            cut(b + 1, DVE_CUT.index(at))
                        if at == DVE_UV and not last:
                            save_uv(b + 1)
                        if at in DVE_NORM and not first:
                            norm(b - 1, DVE_NORM.index(at))
                save_agg(b, first)

            for step in range(4):
                cut(0, step, whole=True)
            save_uv(0, first=True)
            batches(dve, body)
            for step in range(NORM):
                norm(B - 1, step)

        @block.tensor
        def _(pe):
            pe.wait_ge(uv_weights_in, DMA * len(uv_weights))
            pe.wait_ge(ones_set, 1)

            def uv_products(b):
                pe.wait_ge(x_uv_in, DMA * b + DMA)
                if not (isinstance(b, int) and b == 0):
                    pe.wait_ge(uv_saved, b)
                nc.tensor.matmul(uv_ps[:, 0:N], w_v[:], x_uv[:], start=True, stop=True)
                nc.tensor.matmul(uv_ps[:, N:2 * N], w_u[:], x_uv[:], start=True, stop=True
                                 ).then_inc(uv_done, 1)

            def z_half(b, t, half, first=False):
                if half == 0:
                    pair = PAIRS * b + t // 2
                    if first and t < 2:
                        pe.wait_ge(y_ready, t + 1)
                    elif t % 2 == 0:
                        pe.wait_ge(y_ready, pair + 2)
                    elif t // 2 % PAIRS in Y_BY_DVE:
                        pe.wait_ge(y_ready_dve, len(Y_BY_DVE) * b + Y_BY_DVE.index(t // 2) + 1)
                    if t % 2 == 0 and not (first and t < 2):
                        pe.wait_ge(e_ready, TILES * b + t - 1)
                    if t % 2 == 1 and not (first and t < 4):
                        pe.wait_ge(second_agg, 2 * (pair - 1))
                z = zc_ps[:, t // 2 % 2] if t % 2 else zs_ps[:]
                at = t % 2 * TJ + half * HALF
                y = y_ring[:, t // 2 % Y_RING, at:at + HALF, :].rearrange("p j i -> p (j i)")
                mm = nc.tensor.matmul(z[:, half * BANK:(half + 1) * BANK], w_e2_sb[:], y,
                                      start=True, stop=True)
                if half == 1:
                    mm.then_inc(z_ready, 1)

            def spread(b, pair, half, first):
                if pair % (PAIRS // 2) == 0 and half == 0:
                    pe.wait_ge(rows_in[2 * (pair % PAIRS) // PAIRS], DMA * PARTS * (b + 1 + pair // PAIRS))
                if not (first and pair == 0 and half == 0):
                    pe.wait_ge(first_agg, 2 * (PAIRS * b + pair) + (1 if half else -2))
                at = (first_node(2 * (pair % PAIRS)) + half * HALF) * N
                nc.tensor.matmul(a_ps[:], ones[:], adj_rows[:, at:at + BANK], start=True,
                                 stop=True).then_inc(a_ready, 1)

            def node_product(b, layer, last=False):
                if layer == 0:
                    pe.wait_ge(node_weights_in, DMA * len(node_weights))
                    pe.wait_ge(agg_saved, b + 1)
                    if not last:
                        pe.wait_ge(uv_saved, b + 3)
                    nc.tensor.matmul(node_ps, w_n1_sb[:], agg_full[:], start=True, stop=True
                                     ).then_inc(node_mm, 1)
                if layer == 1:
                    pe.wait_ge(node_act, 2 * b + 1)
                    nc.tensor.matmul(node_ps, w_n2_sb[:], node1[:], start=True, stop=True
                                     ).then_inc(node_mm, 1)
                if layer == 2:
                    pe.wait_ge(node_act, 2 * b + 2)
                    pe.wait_ge(x_out_in, DMA * b + DMA)
                    nc.tensor.matmul(node_ps[:, 0:F], x_out[:], w_out_x[:], start=True, stop=False)
                    nc.tensor.matmul(node_ps[:, 0:F], node2[:], w_out_h[:], start=False, stop=True
                                     ).then_inc(node_mm, 1)

            def body(b, first=False, last=False):
                for pair in range(PAIRS):
                    ahead = not (last and pair == PAIRS - 1)
                    t = 2 * (pair + 1)
                    if ahead:
                        for half in range(2):
                            z_half(b, t, half)
                        for half in range(2):
                            z_half(b, t + 1, half, first)
                    if pair % 2 == 0:
                        spread(b, pair, 1, first)
                    if pair % 2 and ahead:
                        spread(b, pair + 1, 0, first)
                    if pair == PE_UV and not last:
                        if not first:
                            pe.wait_ge(agg_saved, b)
                        uv_products(b + 1)
                    if pair in PE_NODE and not first:
                        node_product(b - 1, PE_NODE.index(pair), last)

            uv_products(0)
            pe.wait_ge(edge_weights_in, DMA * len(edge_weights))
            for t in range(2):
                for half in range(2):
                    z_half(0, t, half, first=True)
            spread(0, 0, 0, first=True)
            batches(pe, body)
            for layer in range(3):
                node_product(B - 1, layer, last=True)


def kernel(x, adj, L0_gnn_W_e1, L0_gnn_b_e1, L0_gnn_W_e2, L0_gnn_b_e2, L0_gnn_W_n1, L0_gnn_b_n1,
           L0_gnn_W_n2, L0_gnn_b_n2, L0_gnn_W_out, L0_gnn_b_out):
    import numpy as np
    import concourse.bacc as bacc
    from concourse.bass_utils import run_bass_kernel_spmd

    def laid(a):
        return np.ascontiguousarray(a)

    def column(a):
        return laid(np.asarray(a).reshape(-1, 1))

    x, adj = np.asarray(x), np.asarray(adj)
    arrays = {
        "x": laid(x),
        "x_t": laid(x.transpose(2, 0, 1)),
        "adj_t": laid(adj.transpose(0, 2, 1)),
        "w_e1": laid(L0_gnn_W_e1), "b_e1": column(L0_gnn_b_e1),
        "w_e2": laid(L0_gnn_W_e2), "b_e2": column(L0_gnn_b_e2),
        "w_n1": laid(L0_gnn_W_n1), "b_n1": column(L0_gnn_b_n1),
        "w_n2": laid(L0_gnn_W_n2), "b_n2": column(L0_gnn_b_n2),
        "w_out": laid(L0_gnn_W_out), "b_out": laid(L0_gnn_b_out),
    }
    nc = bacc.Bacc("TRN2", target_bir_lowering=False, num_devices=1)
    args = [nc.dram_tensor(name, a.shape, mybir.dt.from_np(a.dtype), kind="ExternalInput").ap()
            for name, a in arrays.items()]
    out = nc.dram_tensor("out", x.shape, F32, kind="ExternalOutput").ap()
    build_gnn(nc, *args, out)
    result = run_bass_kernel_spmd(nc, [arrays], core_ids=[0])
    return result.results[0]["out"]
```
